# Optimizing a Trainium2 kernel written in Bass

```python
import numpy as np
import jax
import jax.numpy as jnp

def _softmax(x, axis=-1):
    return jax.nn.softmax(x, axis=axis)

def _gelu(x):
    return jax.nn.gelu(x, approximate=True)

def _silu(x):
    return jax.nn.silu(x)

def _sigmoid(x):
    return jax.nn.sigmoid(x)

def _layernorm(x, axis=-1, eps=1e-05):
    m = jnp.mean(x, axis=axis, keepdims=True)
    v = jnp.var(x, axis=axis, keepdims=True)
    return (x - m) / jnp.sqrt(v + eps)

def _scatter_add(tgt, idx, src, axis=0):
    return tgt.at[idx].add(src)

def _segment_sum(src, seg, n):
    return jax.ops.segment_sum(src, seg, n)
kernel_name = 'mk_xattn_seq_d2_seqx_r4_ff131f'

def setup_inputs(seed: int=0):
    np.random.seed(seed)
    _w = jnp.asarray

    def _rec_inputs():
        import jax
        import jax.numpy as jnp
        _rk = jax.random.key(seed)
        x = -0.000929 + 1 * jax.random.normal(jax.random.fold_in(_rk, 1), (4, 512, 256), jnp.float32)
        _lenS = 512 - jax.random.randint(jax.random.fold_in(_rk, 7), (4,), 0, max(1, 512 // 4) + 1, jnp.int32)
        _lenS2 = 64 - jax.random.randint(jax.random.fold_in(_rk, 8), (4,), 0, max(1, 64 // 4) + 1, jnp.int32)
        _ctx_768P = jax.random.normal(jax.random.fold_in(_rk, 11), (4, 16, 192), jnp.float32)
        _ctx_768c = jax.random.dirichlet(jax.random.fold_in(_rk, 511), 0.3 * jnp.ones((16,), jnp.float32), (4, 64))
        _ctx_768t = jnp.einsum('bsk,bkd->bsd', _ctx_768c, _ctx_768P)
        _ctx_768t = _ctx_768t * jax.lax.rsqrt(jnp.mean(jnp.square(_ctx_768t)) + 1e-12) * 0.953939
        ctx_768 = -0.00286756 + 0.998052 * (_ctx_768t + 0.3 * jax.random.normal(jax.random.fold_in(_rk, 611), (4, 64, 192), jnp.float32))
        return (x, ctx_768)
    x, ctx_768 = _rec_inputs()

    def _L0_xattn_setup():
        import jax, jax.numpy as jnp
        import numpy as np
        B_, S_, P_, D_ = (2, 128, 64, 256)
        L_ = 4
        DI_ = 2 * D_
        DS_ = 16
        DC_ = 4
        DR_ = D_ // 16
        PCD_ = 192

        def rmsnorm(x, w, eps=1e-05):
            return x * jax.lax.rsqrt(jnp.mean(x * x, axis=-1, keepdims=True) + eps) * w

        def mamba_block(x, ip_w, cw, cb, xp_w, dtp_w, dtp_b, A_log, Dp, op_w):
            B, S, _ = x.shape
            xz = jnp.einsum('bsd,ed->bse', x, ip_w)
            xi, z = jnp.split(xz, 2, axis=-1)
            xt = xi.transpose(0, 2, 1)
            conv = jax.lax.conv_general_dilated(xt, cw[:, None, :], (1,), [(DC_ - 1, 0)], feature_group_count=DI_) + cb[:, None]
            xi = jax.nn.silu(conv.transpose(0, 2, 1))
            xdbl = jnp.einsum('bse,fe->bsf', xi, xp_w)
            dt, Bm, Cm = jnp.split(xdbl, [DR_, DR_ + DS_], axis=-1)
            dt = jax.nn.softplus(jnp.einsum('bsr,er->bse', dt, dtp_w) + dtp_b)
            A = -jnp.exp(A_log)
            dA = jnp.exp(dt[..., None] * A)
            dBu = dt[..., None] * Bm[:, :, None, :] * xi[..., None]

            def step(h, t):
                da, dbu, c = t
                h = da * h + dbu
                return (h, jnp.einsum('bes,bs->be', h, c))
            h0 = jnp.zeros((B, DI_, DS_), x.dtype)
            _, ys = jax.lax.scan(step, h0, (dA.transpose(1, 0, 2, 3), dBu.transpose(1, 0, 2, 3), Cm.transpose(1, 0, 2)))
            y = ys.transpose(1, 0, 2) + xi * Dp
            y = y * jax.nn.silu(z)
            return jnp.einsum('bse,de->bsd', y, op_w)
        key = jax.random.key(seed)
        ks = jax.random.split(key, 12)
        n = lambda k, s, sc=0.02: jax.random.normal(k, s, dtype=jnp.float32) * sc
        A_log = jnp.log(jnp.broadcast_to(jnp.arange(1, DS_ + 1, dtype=jnp.float32), (L_, DI_, DS_)))
        return {'x': jax.random.normal(ks[0], (B_, S_, D_), dtype=jnp.float32), 'prepend_cond': jax.random.normal(ks[1], (B_, P_, PCD_), dtype=jnp.float32), 'pre_w1': n(ks[2], (PCD_, D_)), 'pre_w2': n(ks[3], (D_, D_)), 'norm_w': jnp.ones((L_, D_), jnp.float32), 'in_proj_w': n(ks[4], (L_, 2 * DI_, D_)), 'conv_w': n(ks[5], (L_, DI_, DC_), 0.1), 'conv_b': jnp.zeros((L_, DI_), jnp.float32), 'x_proj_w': n(ks[6], (L_, DR_ + 2 * DS_, DI_)), 'dt_proj_w': n(ks[7], (L_, DI_, DR_), 0.1), 'dt_proj_b': jax.random.uniform(ks[8], (L_, DI_), jnp.float32, -4.0, -2.0), 'A_log': A_log, 'D_param': jnp.ones((L_, DI_), jnp.float32), 'out_proj_w': n(ks[9], (L_, D_, DI_)), 'final_norm_w': jnp.ones((D_,), jnp.float32)}
    _L0_xattn_all = _L0_xattn_setup()
    _L0_xattn_in = {k: v for k, v in _L0_xattn_all.items() if k in ('pre_w1', 'pre_w2', 'norm_w', 'in_proj_w', 'conv_w', 'conv_b', 'x_proj_w', 'dt_proj_w', 'dt_proj_b', 'A_log', 'D_param', 'out_proj_w', 'final_norm_w')}
    del _L0_xattn_all

    def _L1_xattn_setup():
        import jax, jax.numpy as jnp
        import numpy as np
        DIM1, DIM2, H = (256, 192, 16)
        HID = 4 * DIM1
        EPS = 1e-05

        def layernorm(x, w, b):
            mu = jnp.mean(x, axis=-1, keepdims=True)
            var = jnp.mean((x - mu) ** 2, axis=-1, keepdims=True)
            return (x - mu) * jax.lax.rsqrt(var + EPS) * w + b
        key = jax.random.key(seed)
        ks = jax.random.split(key, 12)
        s1 = 1.0 / np.sqrt(DIM1)
        s2 = 1.0 / np.sqrt(DIM2)
        sh = 1.0 / np.sqrt(HID)
        return {'x': jax.random.normal(ks[0], (4, 256, DIM1), jnp.float32), 'y': jax.random.normal(ks[1], (4, 256, DIM2), jnp.float32), 'ln1_w': jnp.ones((DIM1,), jnp.float32), 'ln1_b': jnp.zeros((DIM1,), jnp.float32), 'ln2_w': jnp.ones((DIM2,), jnp.float32), 'ln2_b': jnp.zeros((DIM2,), jnp.float32), 'ln3_w': jnp.ones((DIM1,), jnp.float32), 'ln3_b': jnp.zeros((DIM1,), jnp.float32), 'Wq': jax.random.uniform(ks[2], (DIM1, DIM1), jnp.float32, -s1, s1), 'Wkv': jax.random.uniform(ks[3], (DIM2, 2 * DIM1), jnp.float32, -s2, s2), 'Wproj': jax.random.uniform(ks[4], (DIM1, DIM1), jnp.float32, -s1, s1), 'bproj': jnp.zeros((DIM1,), jnp.float32), 'W1': jax.random.uniform(ks[5], (DIM1, HID), jnp.float32, -s1, s1), 'b1': jnp.zeros((HID,), jnp.float32), 'W2': jax.random.uniform(ks[6], (HID, DIM1), jnp.float32, -sh, sh), 'b2': jnp.zeros((DIM1,), jnp.float32)}
    _L1_xattn_all = _L1_xattn_setup()
    _L1_xattn_in = {k: v for k, v in _L1_xattn_all.items() if k in ('ln1_w', 'ln1_b', 'ln2_w', 'ln2_b', 'ln3_w', 'ln3_b', 'Wq', 'Wkv', 'Wproj', 'bproj', 'W1', 'b1', 'W2', 'b2')}
    del _L1_xattn_all
    return {'x': x, 'ctx_768': ctx_768, 'L0_xattn_pre_w1': _L0_xattn_in['pre_w1'], 'L0_xattn_pre_w2': _L0_xattn_in['pre_w2'], 'L0_xattn_norm_w': _L0_xattn_in['norm_w'], 'L0_xattn_in_proj_w': _L0_xattn_in['in_proj_w'], 'L0_xattn_conv_w': _L0_xattn_in['conv_w'], 'L0_xattn_conv_b': _L0_xattn_in['conv_b'], 'L0_xattn_x_proj_w': _L0_xattn_in['x_proj_w'], 'L0_xattn_dt_proj_w': _L0_xattn_in['dt_proj_w'], 'L0_xattn_dt_proj_b': _L0_xattn_in['dt_proj_b'], 'L0_xattn_A_log': _L0_xattn_in['A_log'], 'L0_xattn_D_param': _L0_xattn_in['D_param'], 'L0_xattn_out_proj_w': _L0_xattn_in['out_proj_w'], 'L0_xattn_final_norm_w': _L0_xattn_in['final_norm_w'], 'L1_xattn_ln1_w': _L1_xattn_in['ln1_w'], 'L1_xattn_ln1_b': _L1_xattn_in['ln1_b'], 'L1_xattn_ln2_w': _L1_xattn_in['ln2_w'], 'L1_xattn_ln2_b': _L1_xattn_in['ln2_b'], 'L1_xattn_ln3_w': _L1_xattn_in['ln3_w'], 'L1_xattn_ln3_b': _L1_xattn_in['ln3_b'], 'L1_xattn_Wq': _L1_xattn_in['Wq'], 'L1_xattn_Wkv': _L1_xattn_in['Wkv'], 'L1_xattn_Wproj': _L1_xattn_in['Wproj'], 'L1_xattn_bproj': _L1_xattn_in['bproj'], 'L1_xattn_W1': _L1_xattn_in['W1'], 'L1_xattn_b1': _L1_xattn_in['b1'], 'L1_xattn_W2': _L1_xattn_in['W2'], 'L1_xattn_b2': _L1_xattn_in['b2']}

def reference(x, ctx_768, L0_xattn_pre_w1, L0_xattn_pre_w2, L0_xattn_norm_w, L0_xattn_in_proj_w, L0_xattn_conv_w, L0_xattn_conv_b, L0_xattn_x_proj_w, L0_xattn_dt_proj_w, L0_xattn_dt_proj_b, L0_xattn_A_log, L0_xattn_D_param, L0_xattn_out_proj_w, L0_xattn_final_norm_w, L1_xattn_ln1_w, L1_xattn_ln1_b, L1_xattn_ln2_w, L1_xattn_ln2_b, L1_xattn_ln3_w, L1_xattn_ln3_b, L1_xattn_Wq, L1_xattn_Wkv, L1_xattn_Wproj, L1_xattn_bproj, L1_xattn_W1, L1_xattn_b1, L1_xattn_W2, L1_xattn_b2):
    import jax
    import jax.numpy as jnp

    def _L0_xattn_ref(x, prepend_cond, pre_w1, pre_w2, norm_w, in_proj_w, conv_w, conv_b, x_proj_w, dt_proj_w, dt_proj_b, A_log, D_param, out_proj_w, final_norm_w):
        import jax, jax.numpy as jnp
        import numpy as np
        B_, S_, P_, D_ = (2, 128, 64, 256)
        L_ = 4
        DI_ = 2 * D_
        DS_ = 16
        DC_ = 4
        DR_ = D_ // 16
        PCD_ = 192

        def rmsnorm(x, w, eps=1e-05):
            return x * jax.lax.rsqrt(jnp.mean(x * x, axis=-1, keepdims=True) + eps) * w

        def mamba_block(x, ip_w, cw, cb, xp_w, dtp_w, dtp_b, A_log, Dp, op_w):
            B, S, _ = x.shape
            xz = jnp.einsum('bsd,ed->bse', x, ip_w)
            xi, z = jnp.split(xz, 2, axis=-1)
            xt = xi.transpose(0, 2, 1)
            conv = jax.lax.conv_general_dilated(xt, cw[:, None, :], (1,), [(DC_ - 1, 0)], feature_group_count=DI_) + cb[:, None]
            xi = jax.nn.silu(conv.transpose(0, 2, 1))
            xdbl = jnp.einsum('bse,fe->bsf', xi, xp_w)
            dt, Bm, Cm = jnp.split(xdbl, [DR_, DR_ + DS_], axis=-1)
            dt = jax.nn.softplus(jnp.einsum('bsr,er->bse', dt, dtp_w) + dtp_b)
            A = -jnp.exp(A_log)
            dA = jnp.exp(dt[..., None] * A)
            dBu = dt[..., None] * Bm[:, :, None, :] * xi[..., None]

            def step(h, t):
                da, dbu, c = t
                h = da * h + dbu
                return (h, jnp.einsum('bes,bs->be', h, c))
            h0 = jnp.zeros((B, DI_, DS_), x.dtype)
            _, ys = jax.lax.scan(step, h0, (dA.transpose(1, 0, 2, 3), dBu.transpose(1, 0, 2, 3), Cm.transpose(1, 0, 2)))
            y = ys.transpose(1, 0, 2) + xi * Dp
            y = y * jax.nn.silu(z)
            return jnp.einsum('bse,de->bsd', y, op_w)
        p = jax.nn.silu(prepend_cond @ pre_w1) @ pre_w2
        h = jnp.concatenate([p, x], axis=1)
        for l in range(L_):
            h = h + mamba_block(rmsnorm(h, norm_w[l]), in_proj_w[l], conv_w[l], conv_b[l], x_proj_w[l], dt_proj_w[l], dt_proj_b[l], A_log[l], D_param[l], out_proj_w[l])
        h = rmsnorm(h, final_norm_w)
        return h[:, P_:, :]

    def _L1_xattn_ref(x, y, ln1_w, ln1_b, ln2_w, ln2_b, ln3_w, ln3_b, Wq, Wkv, Wproj, bproj, W1, b1, W2, b2):
        import jax, jax.numpy as jnp
        import numpy as np
        DIM1, DIM2, H = (256, 192, 16)
        HID = 4 * DIM1
        EPS = 1e-05

        def layernorm(x, w, b):
            mu = jnp.mean(x, axis=-1, keepdims=True)
            var = jnp.mean((x - mu) ** 2, axis=-1, keepdims=True)
            return (x - mu) * jax.lax.rsqrt(var + EPS) * w + b
        B, N1, C1 = x.shape
        hd = C1 // H
        scale = hd ** (-0.5)
        xn = layernorm(x, ln1_w, ln1_b)
        yn = layernorm(y, ln2_w, ln2_b)
        q = (xn @ Wq).reshape(B, N1, H, hd).transpose(0, 2, 1, 3)
        kv = (yn @ Wkv).reshape(B, y.shape[1], 2, H, hd)
        k = kv[:, :, 0].transpose(0, 2, 1, 3)
        v = kv[:, :, 1].transpose(0, 2, 1, 3)
        attn = jax.nn.softmax(jnp.einsum('bhqd,bhkd->bhqk', q, k) * scale, axis=-1)
        o = jnp.einsum('bhqk,bhkd->bhqd', attn, v).transpose(0, 2, 1, 3).reshape(B, N1, C1)
        x = x + (o @ Wproj + bproj)
        h = jax.nn.gelu(layernorm(x, ln3_w, ln3_b) @ W1 + b1, approximate=False)
        x = x + (h @ W2 + b2)
        return x
    x = _L0_xattn_ref(x, ctx_768, L0_xattn_pre_w1, L0_xattn_pre_w2, L0_xattn_norm_w, L0_xattn_in_proj_w, L0_xattn_conv_w, L0_xattn_conv_b, L0_xattn_x_proj_w, L0_xattn_dt_proj_w, L0_xattn_dt_proj_b, L0_xattn_A_log, L0_xattn_D_param, L0_xattn_out_proj_w, L0_xattn_final_norm_w)
    x = _L1_xattn_ref(x, ctx_768, L1_xattn_ln1_w, L1_xattn_ln1_b, L1_xattn_ln2_w, L1_xattn_ln2_b, L1_xattn_ln3_w, L1_xattn_ln3_b, L1_xattn_Wq, L1_xattn_Wkv, L1_xattn_Wproj, L1_xattn_bproj, L1_xattn_W1, L1_xattn_b1, L1_xattn_W2, L1_xattn_b2)
    return x

_drawn_inputs = setup_inputs


def setup_inputs(seed=0):
    import zlib

    import numpy as np

    out = dict(_drawn_inputs(seed))
    spreads = {'L0_xattn_norm_w': (1.0, 0.6),
     'L0_xattn_conv_b': (0.0, 0.8),
     'L0_xattn_D_param': (1.0, 0.6),
     'L0_xattn_final_norm_w': (1.0, 0.2),
     'L1_xattn_ln1_w': (1.0, 0.6),
     'L1_xattn_ln1_b': (0.0, 2.0),
     'L1_xattn_ln2_w': (1.0, 0.2),
     'L1_xattn_ln2_b': (0.0, 0.278),
     'L1_xattn_ln3_w': (1.0, 0.2),
     'L1_xattn_ln3_b': (0.0, 0.417),
     'L1_xattn_bproj': (0.0, 0.1),
     'L1_xattn_b1': (0.0, 0.1),
     'L1_xattn_b2': (0.0, 0.1)}
    factors = {'L0_xattn_pre_w1': 8.0,
     'L0_xattn_pre_w2': 8.0,
     'L0_xattn_in_proj_w': 5.808,
     'L0_xattn_conv_w': 8.0,
     'L0_xattn_x_proj_w': 8.0,
     'L0_xattn_dt_proj_w': 8.0,
     'L0_xattn_dt_proj_b': 8.0,
     'L0_xattn_A_log': 8.0,
     'L0_xattn_out_proj_w': 5.781}
    for name, (base, spread) in spreads.items():
        noise = np.random.default_rng([zlib.crc32(name.encode()), seed]).standard_normal(out[name].shape)
        drawn = base * np.exp(spread * noise) if base else spread * noise
        out[name] = jnp.asarray(drawn.astype(out[name].dtype))
    for name, factor in factors.items():
        out[name] = (out[name] * factor).astype(out[name].dtype)
    return out
```

```python
from contextlib import ExitStack

import concourse.bass as bass
from concourse import mybir

F32 = mybir.dt.float32
BF16 = mybir.dt.bfloat16
U32 = mybir.dt.uint32
ALU = mybir.AluOpType
ACT = mybir.ActivationFunctionType
AX_X = mybir.AxisListType.X

P = 128
B = 4
S = 512
PRE = 64
T = PRE + S
HALF = T // 2
D = 256
KD = D // P
DC = 192
KC = 2
PC = DC // KC
DI = 2 * D
ET = DI // P
NS = 16
R = D // 16
NX = R + 2 * NS
TAPS = 4
L = 4
UNITS = L * B
W = ET * T
BANK = 512
EPS = 1e-5
SMALL = 2.0 ** -6
HEADS = 16
HD = D // HEADS
GH = 8
HID = 4 * D
KH = HID // P
SLOTS = 4


def mamba_xattn_kernel(nc, xT, ctxT, pre_w1, pre_w2, norm_w, in_w, conv_w, conv_b, x_w, dt_w, dt_b,
                       a_log, d_skip, out_w, fin_w, ln1, ln2, ln3, wq, wkv, wproj, bproj, w1, b1, w2, b2,
                       outT):
    with ExitStack() as top:
        def sb(name, shape, dt=F32, ctx=top):
            return ctx.enter_context(nc.sbuf_tensor(name, shape, dt))

        def sem(name):
            return top.enter_context(nc.semaphore(name))

        h = sb("h", [P, KD, B, T])
        ones = sb("ones", [P, P])
        ident = sb("ident", [P, P])
        mamba_layers(nc, top, h, ones, ident, xT, ctxT, pre_w1, pre_w2, norm_w, in_w, conv_w, conv_b,
                     x_w, dt_w, dt_b, a_log, d_skip, out_w)
        attention_block(nc, top, h, ones, ident, ctxT, fin_w, ln1, ln2, ln3, wq, wkv, wproj, bproj,
                        w1, b1, w2, b2, outT)


def mamba_layers(nc, top, h, ones, ident, xT, ctxT, pre_w1, pre_w2, norm_w, in_w, conv_w, conv_b,
                 x_w, dt_w, dt_b, a_log, d_skip, out_w):
    with ExitStack() as ctx:
        def sb(name, shape, dt=F32):
            return ctx.enter_context(nc.sbuf_tensor(name, shape, dt))

        def psum(name, shape):
            return ctx.enter_context(nc.psum_tensor(name, shape, F32))

        def sem(name):
            return top.enter_context(nc.semaphore(name))

        w_in = sb("w_in", [P, KD, 2 * DI])
        w_out = sb("w_out", [P, ET, D])
        w_x = sb("w_x", [P, ET, NX])
        w_dt = sb("w_dt", [NX, DI])
        NPA = ET * TAPS + ET + ET + KD
        par_all = sb("par_all", [P, L, NPA])
        par = sb("par", [P, NPA])
        dskip = sb("dskip", [P, L, ET])
        nega_all = sb("nega_all", [P, L, ET * NS])
        nega = sb("nega", [P, ET * NS])
        cw = lambda et, k: par[:, et * TAPS + k:et * TAPS + k + 1]
        cb = lambda et: par[:, ET * TAPS + et:ET * TAPS + et + 1]
        dtb = lambda et: par[:, ET * TAPS + ET + et:ET * TAPS + ET + et + 1]
        nw = lambda kd: par[:, ET * TAPS + 2 * ET + kd:ET * TAPS + 2 * ET + kd + 1]
        xc = [sb(f"xc{p}", [P, ET, T]) for p in range(2)]
        sz = [sb(f"sz{p}", [P, ET, T]) for p in range(2)]
        dt = [sb(f"dt{p}", [P, ET, T]) for p in range(2)]
        u = [sb(f"u{p}", [P, ET, T]) for p in range(2)]
        bcs = [sb(f"bcs{p}", [3 * 2 * NS, T], BF16) for p in range(2)]
        xraw = sb("xraw", [P, 2, TAPS - 1 + T])
        wexp = sb("wexp", [P, ET, T])
        ser = sb("ser", [P, ET, T])
        xn = wexp[:, 0:KD, :]
        sq = ser[:, 0:KD, :]
        rstd = sb("rstd", [P, T])
        eps = sb("eps", [P, 1])
        carrier = sb("carrier", [P, 1])
        xdbl = sb("xdbl", [NX, T])
        rest = sb("rest", [2 * NS, T])
        pick = sb("pick", [3 * 2 * NS, 2 * NS], BF16)
        dA = [sb(f"dA{p}", [P, ET, T]) for p in range(2)]
        st = [sb(f"st{p}", [P, ET, T]) for p in range(SLOTS)]
        Bs = [sb(f"Bs{p}", [P, T]) for p in range(2)]
        Cs = [sb(f"Cs{p}", [P, T]) for p in range(SLOTS)]
        flat0 = st[0][:].rearrange("p e t -> p (e t)")
        flat1 = st[1][:].rearrange("p e t -> p (e t)")
        pw1 = flat0[0:PC, 0:KC * D].rearrange("p (k d) -> p k d", k=KC)
        pw2 = flat0[:, 512:512 + KD * D].rearrange("p (k d) -> p k d", k=KD)
        cT = flat1[0:PC, 0:KC * B * PRE].rearrange("p (k t) -> p k t", k=KC)
        p1 = flat1[:, 512:512 + KD * B * PRE].rearrange("p (k t) -> p k t", k=KD)

        y_ps = psum("y_ps", [P, 5 * BANK])
        bc_ps = psum("bc_ps", [P, 2, BANK])
        pj_ps = psum("pj_ps", [P, BANK])

        x_in = sem("x_in")
        pre_in = sem("pre_in")
        par_in = sem("par_in")
        wA_in = sem("wA_in")
        wO_in = sem("wO_in")
        consts = sem("consts")
        zeroed = sem("zeroed")
        pre_mm = sem("pre_mm")
        pre_act = sem("pre_act")
        h_pre = sem("h_pre")
        a_exp = sem("a_exp")
        a_neg = sem("a_neg")
        nega_cur = sem("nega_cur")
        par_cur = sem("par_cur")
        squares = sem("squares")
        ss_mm = sem("ss_mm")
        ln_ms = sem("ln_ms")
        rstd_ok = sem("rstd_ok")
        xn_ok = sem("xn_ok")
        xi_mm = sem("xi_mm")
        xraw_ok = sem("xraw_ok")
        conv_op = sem("conv_op")
        z_mm = sem("z_mm")
        z_copied = sem("z_copied")
        sz_ok = sem("sz_ok")
        xc_ok = sem("xc_ok")
        xp_mm = sem("xp_mm")
        xdbl_ok = sem("xdbl_ok")
        part_op = sem("part_op")
        dt_mm = sem("dt_mm")
        dtx_ok = sem("dtx_ok")
        sp_act = sem("sp_act")
        sp_op = sem("sp_op")
        ser_op = sem("ser_op")
        u_ok = sem("u_ok")
        bc_mm = sem("bc_mm")
        b_ok = sem("b_ok")
        c_ok = sem("c_ok")
        dA_ok = sem("dA_ok")
        dbu_ok = sem("dbu_ok")
        scanned = sem("scanned")
        c_mul = sem("c_mul")
        y_mm = sem("y_mm")
        y_out = sem("y_out")
        gated = sem("gated")
        op_mm = sem("op_mm")
        res_ok = sem("res_ok")
        SP_ACT, SER, PART = 6, 10, 5

        hs = lambda half: slice(HALF * half, HALF * half + HALF)

        def over_units(eng, unit):
            unit(0, 0, True)
            with eng.Fori(0, (UNITS - 2) // 2) as j:
                unit(2 * j + 1, 1, True)
                unit(2 * j + 2, 0, True)
            unit(UNITS - 1, (UNITS - 1) % 2, False)

        block = ctx.enter_context(nc.Block())

        @block.sync
        def _(sp):
            sp.dma_start(cT, ctxT.rearrange("(k p) t -> p k t", p=PC)).then_inc(pre_in, 16)
            sp.dma_start(pw1, pre_w1.rearrange("(k p) d -> p k d", p=PC)).then_inc(pre_in, 16)
            sp.dma_start(pw2, pre_w2.rearrange("(k p) d -> p k d", p=P)).then_inc(pre_in, 16)
            o = 0
            for src, n in ((conv_w, ET * TAPS), (conv_b, ET), (dt_b, ET), (norm_w, KD)):
                sp.dma_start(par_all[:, :, o:o + n], src.rearrange("p (l e) -> p l e", l=L)).then_inc(par_in, 16)
                o += n
            sp.dma_start(h[:, 0, :, PRE:T], xT[0:P].rearrange("p (b t) -> p b t", b=B)).then_inc(x_in, 16)
            sp.dma_start(h[:, 1, :, PRE:T], xT[P:D].rearrange("p (b t) -> p b t", b=B)).then_inc(x_in, 16)

            def load_a(l):
                sp.dma_start(w_in[:], in_w[l].rearrange("(k p) e -> p k e", p=P)).then_inc(wA_in, 16)
                sp.dma_start(w_x[:], x_w[l].rearrange("(k p) e -> p k e", p=P)).then_inc(wA_in, 16)
                sp.dma_start(w_dt[2 * NS:NX, :], dt_w[l]).then_inc(wA_in, 16)

            def load_o(l):
                sp.dma_start(w_out[:], out_w[l].rearrange("(k p) e -> p k e", p=P)).then_inc(wO_in, 16)

            load_a(0)
            sp.dma_start(nega_all[:], a_log.rearrange("p (l e) -> p l e", l=L)).then_inc(par_in, 16)
            sp.dma_start(dskip[:], d_skip.rearrange("p (l e) -> p l e", l=L)).then_inc(par_in, 16)
            load_o(0)
            with sp.Fori(1, L) as l:
                sp.wait_ge(dt_mm, 2 * ET * B * l)
                sp.wait_ge(z_mm, 2 * ET * B * l)
                load_a(l)
                sp.wait_ge(op_mm, 2 * KD * B * l)
                load_o(l)

        @block.gpsimd
        def _(pool):
            nc.gpsimd.memset(ident[:], 0.0).then_inc(consts, 1)
            nc.gpsimd.memset(pick[:], 0.0).then_inc(consts, 1)
            pool.wait_ge(consts, 2)
            nc.gpsimd.affine_select(out=ident[:], in_=ident[:], compare_op=ALU.not_equal, fill=1.0, base=0,
                                    pattern=[[-1, P]], channel_multiplier=1).then_inc(consts, 1)
            for q in range(3):
                part = pick[2 * NS * q:2 * NS * (q + 1), :]
                pool.wait_ge(consts, 3 + q)
                nc.gpsimd.affine_select(out=part, in_=part, compare_op=ALU.not_equal, fill=1.0, base=0,
                                        pattern=[[-1, 2 * NS]], channel_multiplier=1).then_inc(consts, 1)

            def unit(i, par_, ahead):
                for n in range(NS):
                    s = n % SLOTS
                    pool.wait_ge(c_ok, NS * i + n + 1)
                    pool.wait_ge(scanned, NS * i + n + 1)
                    nc.gpsimd.tensor_tensor(st[s][:], st[s][:], Cs[s][:].unsqueeze(1).broadcast_to([P, ET, T]),
                                            ALU.mult).then_inc(c_mul, 1)

            over_units(pool, unit)

        @block.tensor
        def _(pe):
            def chunk_free(k, m):
                kind, c = m
                if kind == "ss":
                    if c == 0:
                        pe.wait_ge(dtx_ok, 2 * ET * k)
                    else:
                        pe.wait_ge(ln_ms, 2 * k + c)
                elif kind == "xi":
                    if c == 0:
                        pe.wait_ge(ln_ms, 2 * k + 2)
                        pe.wait_ge(res_ok, 2 * KD * (k - 1)) if not (isinstance(k, int) and k < 2) else None
                    else:
                        pe.wait_ge(xraw_ok, 2 * ET * k + c)
                elif kind == "z":
                    pe.wait_ge(z_copied if c else xraw_ok, 2 * ET * k + (c or 2 * ET))
                elif kind == "xp":
                    pe.wait_ge(xdbl_ok if c else z_copied, 2 * k + c if c else 2 * ET * k + 2 * ET)
                elif kind == "dt":
                    pe.wait_ge(dtx_ok if c else xdbl_ok, 2 * ET * k + c if c else 2 * k + 2)

            def proj_chunk(k, p, m):
                kind, c = m
                half = c % 2
                et = c // 2
                chunk_free(k, m)
                o = pj_ps[:, 0:HALF]
                if kind == "ss":
                    if c == 0:
                        pe.wait_ge(squares, k + 1)
                    for kd in range(KD):
                        mm = nc.tensor.matmul(o, ones[:], sq[:, kd, hs(half)], start=kd == 0, stop=kd == KD - 1)
                    mm.then_inc(ss_mm, 1)
                elif kind in ("xi", "z"):
                    if m == ("xi", 0):
                        pe.wait_ge(xn_ok, k + 1)
                        pe.wait_ge(wA_in, 48 * (k // B + 1))
                    col = (et + (ET if kind == "z" else 0)) * P
                    for kd in range(KD):
                        mm = nc.tensor.matmul(o, w_in[:, kd, col:col + P], xn[:, kd, hs(half)],
                                              start=kd == 0, stop=kd == KD - 1)
                    mm.then_inc(xi_mm if kind == "xi" else z_mm, 1)
                elif kind == "xp":
                    if c == 0:
                        pe.wait_ge(xc_ok, k + 1)
                    for e in range(ET):
                        mm = nc.tensor.matmul(pj_ps[0:NX, 0:HALF], w_x[:, e, :], xc[p][:, e, hs(half)],
                                              start=e == 0, stop=e == ET - 1)
                    mm.then_inc(xp_mm, 1)
                elif kind == "dt":
                    nc.tensor.matmul(o, w_dt[2 * NS:NX, et * P:et * P + P], xdbl[2 * NS:NX, hs(half)],
                                     start=True, stop=True).then_inc(dt_mm, 1)

            def out_chunk(m, p, c, bank_free):
                if c == 0:
                    pe.wait_ge(gated, m + 1)
                    pe.wait_ge(wO_in, 16 * (m // B + 1))
                    bank_free()
                else:
                    pe.wait_ge(res_ok, 2 * KD * m + c)
                kd, half = c // 2, c % 2
                for e in range(ET):
                    mm = nc.tensor.matmul(pj_ps[:, 0:HALF], w_out[:, e, kd * P:kd * P + P], xc[p][:, e, hs(half)],
                                          start=e == 0, stop=e == ET - 1)
                mm.then_inc(op_mm, 1)

            def spread(i, p, n, which):
                if which == 0:
                    if n == 0:
                        pe.wait_ge(part_op, PART * (i + 1))
                    if not (isinstance(i, int) and i == 0 and n == 0):
                        pe.wait_ge(c_ok, NS * i + n)
                else:
                    pe.wait_ge(b_ok, NS * i + n + 1)
                row = which * NS + n
                for half in range(2):
                    mm = nc.tensor.matmul(bc_ps[:, half, 0:HALF], pick[:, row:row + 1].broadcast_to([96, P]),
                                          bcs[p][:, hs(half)], start=True, stop=True)
                mm.then_inc(bc_mm, 1)

            def state_sum(i, n, cs):
                if n == 0 and 0 in cs:
                    if not (isinstance(i, int) and i == 0):
                        pe.wait_ge(y_out, i)
                if 0 in cs:
                    pe.wait_ge(c_mul, NS * i + n + 1)
                s = st[n % SLOTS][:].rearrange("p e t -> p (e t)")
                for c in cs:
                    lo, hi = c * BANK, min(W, (c + 1) * BANK)
                    mm = nc.tensor.matmul(y_ps[:, lo:hi], ident[:], s[:, lo:hi], start=n == 0, stop=n == NS - 1)
                if 4 in cs:
                    mm.then_inc(y_mm, 1)

            plan = [[] for _ in range(NS)]
            for step, kind, cs in ((0, "ss", (0, 1)), (2, "op", (0, 1, 2)), (3, "op", (3,)), (3, "xi", (0, 1)),
                                   (4, "xi", (2, 3, 4)), (5, "xi", (5, 6, 7)), (6, "z", (0, 1, 2)),
                                   (7, "z", (3, 4, 5)), (8, "z", (6, 7)), (9, "xp", (0, 1)),
                                   (11, "dt", (0, 1, 2)), (12, "dt", (3, 4, 5)), (13, "dt", (6, 7))):
                plan[step] += [(kind, c) for c in cs]

            def unit(i, p, ahead):
                q = 1 - p
                for n in range(NS):
                    todo = [m for m in plan[n] if ahead or m[0] == "op"]
                    if isinstance(i, int) and i == 0:
                        todo = [m for m in todo if m[0] != "op"]
                    free = (lambda: pe.wait_ge(ln_ms, 2 * i + 4)) if ahead else \
                        (lambda: pe.wait_ge(dtx_ok, 2 * ET * UNITS))
                    todo = [(lambda m=m: out_chunk(i - 1, q, m[1], free)) if m[0] == "op"
                            else (lambda m=m: proj_chunk(i + 1, q, m)) for m in todo]
                    todo += [lambda: None] * (3 - len(todo))
                    last = n == NS - 1
                    if not last:
                        spread(i, p, n + 1, 0)
                    elif ahead:
                        spread(i + 1, q, 0, 0)
                    prev = (i, n - 1) if n else (i - 1, NS - 1)
                    first = n == 0 and isinstance(i, int) and i == 0
                    if not first:
                        state_sum(*prev, (0, 1))
                    todo[0]()
                    if not last:
                        spread(i, p, n + 1, 1)
                    elif ahead:
                        spread(i + 1, q, 0, 1)
                    if not first:
                        state_sum(*prev, (2, 3))
                    todo[1]()
                    if not first:
                        state_sum(*prev, (4,))
                    todo[2]()

            pe.wait_ge(pre_in, 48)
            for m in range(KD):
                for k in range(KC):
                    mm = nc.tensor.matmul(y_ps[:, m * BANK:m * BANK + B * PRE], pw1[:, k, m * P:m * P + P],
                                          cT[:, k, :], start=k == 0, stop=k == KC - 1)
                mm.then_inc(pre_mm, 1)
            pe.wait_ge(pre_act, KD)
            for m in range(KD):
                for k in range(KD):
                    mm = nc.tensor.matmul(y_ps[:, (2 + m) * BANK:(2 + m) * BANK + B * PRE],
                                          pw2[:, k, m * P:m * P + P], p1[:, k, :],
                                          start=k == 0, stop=k == KD - 1)
                mm.then_inc(pre_mm, 1)
            pe.wait_ge(zeroed, 5)
            pe.wait_ge(consts, 6)
            for step in plan:
                for m in step:
                    if m[0] != "op":
                        proj_chunk(0, 0, m)
            spread(0, 0, 0, 0)
            spread(0, 0, 0, 1)
            over_units(pe, unit)
            state_sum(UNITS - 1, NS - 1, range(5))
            for c in range(2 * KD):
                out_chunk(UNITS - 1, (UNITS - 1) % 2, c,
                          lambda: pe.wait_ge(res_ok, 2 * KD * (UNITS - 1)))

        @block.scalar
        def _(act):
            def take_chunk(k, p, m):
                kind, c = m
                half, et = c % 2, c // 2
                src = pj_ps[:, 0:HALF]
                if kind == "ss":
                    act.wait_ge(ss_mm, 2 * k + c + 1)
                    if c == 0 and not (isinstance(k, int) and k == 0):
                        act.wait_ge(xn_ok, k)
                    nc.scalar.activation(rstd[:, hs(half)], src, ACT.Ln, bias=eps[:, 0:1]).then_inc(ln_ms, 1)
                elif kind == "xi":
                    act.wait_ge(xi_mm, 2 * ET * k + c + 1)
                    if half == 0:
                        if et >= 2:
                            act.wait_ge(conv_op, TAPS * (ET * k + et - 1))
                        elif not (isinstance(k, int) and k == 0):
                            act.wait_ge(conv_op, TAPS * (ET * k - 2 + et + 1))
                    nc.scalar.activation(xraw[:, et % 2, TAPS - 1 + half * HALF:TAPS - 1 + (half + 1) * HALF],
                                         src, ACT.Copy).then_inc(xraw_ok, 1)
                elif kind == "z":
                    act.wait_ge(z_mm, 2 * ET * k + c + 1)
                    if c == 0 and not (isinstance(k, int) and k < 2):
                        act.wait_ge(gated, k - 1)
                    nc.scalar.activation(sz[p][:, et, hs(half)], src, ACT.Copy).then_inc(z_copied, 1)
                elif kind == "xp":
                    act.wait_ge(xp_mm, 2 * k + c + 1)
                    if c == 0 and not (isinstance(k, int) and k == 0):
                        act.wait_ge(part_op, PART * k)
                        act.wait_ge(dt_mm, 2 * ET * k)
                    nc.scalar.activation(xdbl[:, hs(half)], pj_ps[0:NX, 0:HALF], ACT.Copy).then_inc(xdbl_ok, 1)
                elif kind == "dt":
                    act.wait_ge(dt_mm, 2 * ET * k + c + 1)
                    if c == 0 and not (isinstance(k, int) and k < 2):
                        act.wait_ge(dbu_ok, NS * (k - 1))
                    nc.scalar.activation(u[p][:, et, hs(half)], src, ACT.Identity,
                                         bias=dtb(et)).then_inc(dtx_ok, 1)

            def square(k, bsel):
                if not (isinstance(k, int) and k < 2):
                    act.wait_ge(scanned, NS * (k - 2) + 5)
                if not (isinstance(k, int) and k == 0):
                    act.wait_ge(sp_op, 2 * k)
                nc.scalar.activation(sq, h[:, :, bsel, :], ACT.Square).then_inc(squares, 1)

            def finish_rstd(k):
                act.wait_ge(ln_ms, 2 * k + 2)
                nc.scalar.activation(rstd[:], rstd[:], ACT.Exp, scale=-0.5).then_inc(rstd_ok, 1)

            def silus(k, p):
                act.wait_ge(z_copied, 2 * ET * k + 2 * ET)
                nc.scalar.activation(sz[p][:], sz[p][:], ACT.Silu).then_inc(sz_ok, 1)
                act.wait_ge(conv_op, TAPS * ET * (k + 1))
                nc.scalar.activation(xc[p][:], xc[p][:], ACT.Silu).then_inc(xc_ok, 1)

            def softplus(k, p, g):
                e = slice(2 * g, 2 * g + 2)
                act.wait_ge(dtx_ok, 2 * ET * k + ET * (g + 1))
                if g == 0:
                    act.wait_ge(z_mm, 2 * ET * (k + 1))
                nc.scalar.activation(wexp[:, e, :], u[p][:, e, :], ACT.Abs).then_inc(sp_act, 1)
                act.wait_ge(sp_act, SP_ACT * k + 3 * g + 1)
                nc.scalar.activation(wexp[:, e, :], wexp[:, e, :], ACT.Exp, scale=-1.0).then_inc(sp_act, 1)
                act.wait_ge(sp_act, SP_ACT * k + 3 * g + 2)
                nc.scalar.activation(dt[p][:, e, :], wexp[:, e, :], ACT.Ln, bias=1.0).then_inc(sp_act, 1)

            def decay(i, p, n, ets):
                if 0 in ets:
                    if n == 0:
                        act.wait_ge(sp_op, 2 * (i + 1))
                        if not (isinstance(i, int) and i == 0):
                            act.wait_ge(dA_ok, NS * i)
                        layer = i // B
                        nc.scalar.activation(nega[:], nega_all[:, layer, :], ACT.Copy).then_inc(nega_cur, 1)
                        act.wait_ge(nega_cur, i + 1)
                    if not (isinstance(i, int) and i == 0 and n < 2):
                        act.wait_ge(scanned, NS * i + n - 1)
                for et in ets:
                    a = nc.scalar.activation(dA[n % 2][:, et, 1:T], dt[p][:, et, 1:T], ACT.Exp,
                                             scale=nega[:, et * NS + n:et * NS + n + 1])
                if ET - 1 in ets:
                    a.then_inc(dA_ok, 1)

            def take_row(i, n, which):
                act.wait_ge(bc_mm, 2 * (NS * i + n) + which + 1)
                if which == 0:
                    if not (isinstance(i, int) and i == 0 and n < 2):
                        act.wait_ge(dbu_ok, NS * i + n - 1)
                    dst, ok = Bs[n % 2], b_ok
                else:
                    if not (isinstance(i, int) and i == 0 and n < SLOTS):
                        act.wait_ge(c_mul, NS * i + n - SLOTS + 1)
                    dst, ok = Cs[n % SLOTS], c_ok
                nc.scalar.activation(dst[:].rearrange("p (a c) -> p a c", a=2), bc_ps[:, :, 0:HALF],
                                     ACT.Copy).then_inc(ok, 1)

            evac = [[] for _ in range(NS)]
            for step, kind, cs in ((0, "ss", (0, 1)), (3, "xi", (0, 1)),
                                   (4, "xi", (2, 3, 4)), (5, "xi", (5, 6, 7)), (6, "z", (0, 1, 2)),
                                   (7, "z", (3, 4, 5)), (8, "z", (6, 7)), (9, "xp", (0, 1)),
                                   (11, "dt", (0, 1, 2)), (12, "dt", (3, 4, 5)), (13, "dt", (6, 7))):
                evac[step] += [(kind, c) for c in cs]

            def after_step(k, p, n):
                if n == 0:
                    finish_rstd(k)
                elif n == 8:
                    silus(k, p)
                elif n == 12:
                    softplus(k, p, 0)
                elif n == 13:
                    softplus(k, p, 1)

            def unit(i, p, ahead):
                q = 1 - p
                for n in range(NS):
                    nxt = (i, p, n + 1) if n < NS - 1 else (i + 1, q, 0)
                    go = n < NS - 1 or ahead
                    if n == 0 and ahead:
                        square(i + 1, (i + 1) % B)
                    todo = [(lambda m=m: take_chunk(i + 1, q, m)) for m in evac[n]] if ahead else []
                    todo += [lambda: None] * (3 - len(todo))
                    if go:
                        take_row(nxt[0], nxt[2], 0)
                        decay(*nxt, (0, 1))
                    todo[0]()
                    if go:
                        take_row(nxt[0], nxt[2], 1)
                        decay(*nxt, (2,))
                    todo[1]()
                    if go:
                        decay(*nxt, (3,))
                    todo[2]()
                    if ahead:
                        after_step(i + 1, q, n)

            for m in range(KD):
                act.wait_ge(pre_mm, m + 1)
                nc.scalar.activation(p1[:, m, :], y_ps[:, m * BANK:m * BANK + B * PRE],
                                     ACT.Silu).then_inc(pre_act, 1)
            act.wait_ge(par_in, 96)
            nc.scalar.activation(nega_all[:], nega_all[:], ACT.Exp).then_inc(a_exp, 1)
            act.wait_ge(h_pre, KD)
            act.wait_ge(x_in, 32)
            act.wait_ge(zeroed, 5)
            square(0, 0)
            for n, step in enumerate(evac):
                for m in step:
                    take_chunk(0, 0, m)
                after_step(0, 0, n)
            act.wait_ge(a_neg, 1)
            take_row(0, 0, 0)
            decay(0, 0, 0, (0, 1, 2, 3))
            take_row(0, 0, 1)
            over_units(act, unit)

        @block.vector
        def _(dve):
            def copy_params(k):
                if not (isinstance(k, int) and k == 0):
                    dve.wait_ge(dtx_ok, 2 * ET * k)
                nc.vector.tensor_copy(par[:], par_all[:, k // B, :]).then_inc(par_cur, 1)
                dve.wait_ge(par_cur, k + 1)

            def norm(k):
                dve.wait_ge(rstd_ok, k + 1)
                for kd in range(KD):
                    a = nc.vector.scalar_tensor_tensor(out=xn[:, kd, :], in0=h[:, kd, k % B, :], scalar=nw(kd),
                                                       in1=rstd[:], op0=ALU.mult, op1=ALU.mult)
                a.then_inc(xn_ok, 1)

            def conv(k, p, et):
                if et == 0 and not (isinstance(k, int) and k < 2):
                    dve.wait_ge(op_mm, 2 * KD * (k - 1))
                dve.wait_ge(xraw_ok, 2 * (ET * k + et) + 2)
                base = TAPS * (ET * k + et)
                nc.vector.tensor_scalar(xc[p][:, et, :], xraw[:, et % 2, TAPS - 1:TAPS - 1 + T],
                                        cw(et, TAPS - 1), cb(et), ALU.mult, ALU.add).then_inc(conv_op, 1)
                for j in range(1, TAPS):
                    dve.wait_ge(conv_op, base + j)
                    s = TAPS - 1 - j
                    nc.vector.scalar_tensor_tensor(out=xc[p][:, et, :], in0=xraw[:, et % 2, s:s + T],
                                                   scalar=cw(et, s), in1=xc[p][:, et, :],
                                                   op0=ALU.mult, op1=ALU.add).then_inc(conv_op, 1)

            def split(k, p):
                n = 2 * NS
                dve.wait_ge(xdbl_ok, 2 * k + 2)
                if not (isinstance(k, int) and k < 2):
                    dve.wait_ge(c_ok, NS * (k - 1))
                part = [bcs[p][n * j:n * j + n, :] for j in range(3)]
                src = xdbl[0:n, :]
                for j in range(3):
                    nc.vector.tensor_copy(part[j], src).then_inc(part_op, 1)
                    dve.wait_ge(part_op, PART * k + 2 * j + 1)
                    if j < 2:
                        nc.vector.tensor_tensor(rest[:], src, part[j], ALU.subtract).then_inc(part_op, 1)
                        dve.wait_ge(part_op, PART * k + 2 * j + 2)
                        src = rest[:]

            def softplus(k, p, g):
                e = slice(2 * g, 2 * g + 2)
                w, s, l, x = wexp[:, e, :], ser[:, e, :], dt[p][:, e, :], u[p][:, e, :]
                dve.wait_ge(sp_act, SP_ACT * k + 3 * g + 3)
                nc.vector.tensor_scalar(s, w, 1.0 / 3.0, -0.5, ALU.mult, ALU.add).then_inc(ser_op, 1)
                dve.wait_ge(ser_op, SER * k + 5 * g + 1)
                nc.vector.tensor_tensor(s, s, w, ALU.mult).then_inc(ser_op, 1)
                dve.wait_ge(ser_op, SER * k + 5 * g + 2)
                nc.vector.scalar_tensor_tensor(out=s, in0=s, scalar=1.0, in1=w, op0=ALU.add,
                                               op1=ALU.mult).then_inc(ser_op, 1)
                dve.wait_ge(ser_op, SER * k + 5 * g + 3)
                nc.vector.tensor_scalar(w, w, SMALL, None, ALU.is_lt).then_inc(ser_op, 1)
                dve.wait_ge(ser_op, SER * k + 5 * g + 4)
                nc.vector.memset(carrier[:], 0.0)
                nc.vector.copy_predicated(l, w.bitcast(U32), s).then_inc(ser_op, 1)
                dve.wait_ge(ser_op, SER * k + 5 * g + 5)
                nc.vector.scalar_tensor_tensor(out=l, in0=x, scalar=0.0, in1=l, op0=ALU.max,
                                               op1=ALU.add).then_inc(sp_op, 1)
                dve.wait_ge(sp_op, 2 * k + g + 1)
                nc.vector.tensor_tensor(x, l, xc[p][:, e, :], ALU.mult).then_inc(u_ok, 1)

            def y_evac(m, p):
                dve.wait_ge(y_mm, NS * (m + 1))
                for et in range(ET):
                    a = nc.vector.scalar_tensor_tensor(out=xc[p][:, et, :], in0=xc[p][:, et, :],
                                                       scalar=dskip[:, m // B, et:et + 1],
                                                       in1=y_ps[:, et * T:et * T + T], op0=ALU.mult, op1=ALU.add)
                a.then_inc(y_out, 1)
                dve.wait_ge(y_out, m + 1)
                dve.wait_ge(sz_ok, m + 1)
                nc.vector.tensor_tensor(xc[p][:], xc[p][:], sz[p][:], ALU.mult).then_inc(gated, 1)

            def residual(m, c):
                dve.wait_ge(op_mm, 2 * KD * m + c + 1)
                kd, half = c // 2, c % 2
                t = h[:, kd, m % B, hs(half)]
                nc.vector.tensor_tensor(t, t, pj_ps[:, 0:HALF], ALU.add).then_inc(res_ok, 1)

            def unit(i, p, ahead):
                q = 1 - p
                first = isinstance(i, int) and i == 0
                for n in range(NS):
                    s = n % SLOTS
                    dve.wait_ge(b_ok, NS * i + n + 1)
                    if n == 0:
                        dve.wait_ge(u_ok, 2 * (i + 1))
                    if not (first and n < SLOTS):
                        dve.wait_ge(y_mm, NS * i + n - SLOTS + 1)
                    nc.vector.tensor_tensor(st[s][:], u[p][:], Bs[n % 2][:].unsqueeze(1).broadcast_to([P, ET, T]),
                                            ALU.mult).then_inc(dbu_ok, 1)
                    if n == 0:
                        if ahead:
                            copy_params(i + 1)
                    if n == 1 and not first:
                        y_evac(i - 1, q)
                    dve.wait_ge(dA_ok, NS * i + n + 1)
                    dve.wait_ge(dbu_ok, NS * i + n + 1)
                    f = st[s][:].rearrange("p e t -> p (e t)")
                    nc.vector.tensor_tensor_scan(f, dA[n % 2][:].rearrange("p e t -> p (e t)"), f, 0.0,
                                                 ALU.mult, ALU.add).then_inc(scanned, 1)
                    if not first and n in (2, 3):
                        for c in ((0, 1, 2), (3,))[n - 2]:
                            residual(i - 1, c)
                    if ahead:
                        if n == 0:
                            norm(i + 1)
                        for et in {3: (0,), 4: (1,), 5: (2, 3)}.get(n, ()):
                            conv(i + 1, q, et)
                        if n == 9:
                            split(i + 1, q)
                        if n in (13, 14):
                            softplus(i + 1, q, n - 13)

            nc.vector.memset(ones[:], 1.0 / D).then_inc(zeroed, 1)
            nc.vector.memset(xraw[:, :, 0:TAPS - 1], 0.0).then_inc(zeroed, 1)
            nc.vector.memset(dA[0][:, :, 0:1], 0.0).then_inc(zeroed, 1)
            nc.vector.memset(dA[1][:, :, 0:1], 0.0).then_inc(zeroed, 1)
            nc.vector.memset(eps[:], EPS).then_inc(zeroed, 1)
            dve.wait_ge(zeroed, 5)
            for m in range(KD):
                dve.wait_ge(pre_mm, KD + m + 1)
                nc.vector.tensor_copy(h[:, m, :, 0:PRE],
                                      y_ps[:, (2 + m) * BANK:(2 + m) * BANK + B * PRE].rearrange(
                                          "p (b t) -> p b t", b=B)).then_inc(h_pre, 1)
            dve.wait_ge(a_exp, 1)
            nc.vector.tensor_scalar(nega_all[:], nega_all[:], -1.0, None, ALU.mult).then_inc(a_neg, 1)
            dve.wait_ge(par_in, 96)
            dve.wait_ge(x_in, 32)
            copy_params(0)
            norm(0)
            for et in range(ET):
                conv(0, 0, et)
            split(0, 0)
            softplus(0, 0, 0)
            softplus(0, 0, 1)
            over_units(dve, unit)
            y_evac(UNITS - 1, (UNITS - 1) % 2)
            for c in range(2 * KD):
                residual(UNITS - 1, c)


def attention_block(nc, top, h, ones, ident, ctxT, fin_w, ln1, ln2, ln3, wq, wkv, wproj, bproj,
                    w1, b1, w2, b2, outT):
    with ExitStack() as ctx:
        def sb(name, shape, dt=F32):
            return ctx.enter_context(nc.sbuf_tensor(name, shape, dt))

        def psum(name, shape):
            return ctx.enter_context(nc.psum_tensor(name, shape, F32))

        def sem(name):
            return top.enter_context(nc.semaphore(name))

        CT = B * PRE
        QT = S // P
        G = D // P
        PAIRS = HEADS // 2
        PG = GH // 2
        SCALE = HD ** -0.5

        wq_s = sb("wq_s", [P, KD, D])
        wkv_s = sb("wkv_s", [PC, KC, 2 * D])
        wp_s = sb("wp_s", [P, KD, D])
        w1_s = sb("w1_s", [P, KD, HID])
        w2_s = sb("w2_s", [P, KH, D])
        fin_s = sb("fin_s", [P, KD])
        ln1_s = sb("ln1_s", [P, 2 * KD])
        ln3_s = sb("ln3_s", [P, 2 * KD])
        ln2_s = sb("ln2_s", [PC, 2 * KC])
        bp_s = sb("bp_s", [P, KD])
        b1_s = sb("b1_s", [P, KH])
        b2_s = sb("b2_s", [P, KD])
        eps = sb("eps_l1", [P, 1])
        ones_c = sb("ones_c", [PC, P])
        cT = sb("cT_l1", [PC, KC, CT])
        cq = sb("cq", [PC, KC, CT])
        crs = sb("crs", [PC, CT])
        kT = sb("kT", [P, G, CT])
        vdup = sb("vdup", [P, B, D])
        kmask = sb("kmask", [P, GH, PRE])
        kblk = sb("kblk", [P, G, GH, PRE])
        vblk = sb("vblk", [P, G, PG * 160])
        sq = sb("sq_l1", [P, KD, S])
        rs = sb("rs", [P, S])
        x1 = sb("x1", [P, KD, S])
        xm = sb("xm", [P, KD, S])
        xn = sb("xn_l1", [P, KD, S])
        qT = sb("qT", [P, G, S])
        ex = [sb(f"ex{p}", [P, HEADS, PRE]) for p in range(2)]
        mx = [sb(f"mx{p}", [P, HEADS]) for p in range(2)]
        den = [sb(f"den{p}", [P, HEADS]) for p in range(2)]
        aT = sb("aT", [P, PAIRS, S])
        oT = sb("oT", [P, KD, S])
        hT = sb("hT", [P, KH, S])
        res = sb("res", [P, KD, S])

        pj = [psum(f"pj{p}", [P, BANK]) for p in range(2)]
        sc = [psum(f"sc{p}", [P, HEADS, PRE]) for p in range(2)]
        tp = psum("tp", [P, PAIRS, P])

        w_in = sem("l1_w_in")
        c_in = sem("l1_c_in")
        consts = sem("l1_consts")
        zeroed = sem("l1_zeroed")
        c_mm = sem("c_mm")
        c_act = sem("c_act")
        c_dve = sem("c_dve")
        kv_out = sem("kv_out")
        pj_mm = sem("pj_mm")
        by_act = sem("by_act")
        by_dve = sem("by_dve")
        kblk_ok = sem("kblk_ok")
        vblk_ok = sem("vblk_ok")
        sc_mm = sem("sc_mm")
        shifted = sem("shifted")
        mx_ok = sem("mx_ok")
        ex_ok = sem("ex_ok")
        den_ok = sem("den_ok")
        rden_ok = sem("rden_ok")
        att_ok = sem("att_ok")
        tp_mm = sem("tp_mm")
        aT_ok = sem("aT_ok")
        sq_ok = sem("sq_ok")
        xh_ok = sem("xh_ok")
        xn_ok = sem("l1_xn_ok")
        rs_ok = sem("rs_ok")
        stored = sem("stored")

        USES = ([("ms", "act"), ("mean1", "dve"), ("var1", "act")] + [(f"q{m}", "act") for m in range(G)]
                + [(f"o{g}", "act") for g in range(G)] + [(f"p{m}", "dve") for m in range(KD)]
                + [("mean3", "dve"), ("var3", "act")] + [(f"h{m}", "act") for m in range(KH)]
                + [(f"y{m}", "dve") for m in range(KD)] + [("pad", None)])
        NAMES = [u for u, _ in USES]
        N_USES = len(USES) - 1
        N_ACT = sum(e == "act" for _, e in USES)
        N_DVE = sum(e == "dve" for _, e in USES)
        assert len(USES) % 2 == 0

        def bank(use):
            return pj[NAMES.index(use) % 2]

        def taken(b, use):
            at = NAMES.index(use)
            who = USES[at][1]
            n = sum(e == who for _, e in USES[:at + 1])
            return (by_act, N_ACT * b + n) if who == "act" else (by_dve, N_DVE * b + n)

        def before(use):
            at = NAMES.index(use) - 2
            ago = 0 if at >= 0 else 1
            at %= len(USES)
            if USES[at][1] is None:
                at -= 2
            return NAMES[at], ago

        def filled(b, use):
            return N_USES * b + NAMES.index(use) + 1

        block = ctx.enter_context(nc.Block())

        @block.sync
        def _(sp):
            sp.dma_start(cT[:], ctxT.rearrange("(k p) t -> p k t", p=PC)).then_inc(c_in, 16)
            sp.dma_start(ln2_s[:], ln2).then_inc(c_in, 16)
            sp.dma_start(wkv_s[:], wkv.rearrange("(k p) e -> p k e", p=PC)).then_inc(c_in, 16)
            for t, src in ((fin_s, fin_w), (ln1_s, ln1), (ln3_s, ln3), (bp_s, bproj), (b1_s, b1), (b2_s, b2)):
                sp.dma_start(t[:], src).then_inc(w_in, 16)
            for t, src in ((wq_s, wq), (wp_s, wproj), (w1_s, w1), (w2_s, w2)):
                sp.dma_start(t[:], src.rearrange("(k p) e -> p k e", p=P)).then_inc(w_in, 16)
            with sp.Fori(0, B) as b:
                for kd in range(KD):
                    sp.wait_ge(*taken(b, f"y{kd}"))
                    sp.dma_start(outT[kd, b], res[:, kd, :]).then_inc(stored, 16)
            sp.wait_ge(stored, 16 * KD * B)

        @block.gpsimd
        def _(pool):
            nc.gpsimd.memset(kmask[:], 1.0).then_inc(consts, 1)
            nc.gpsimd.memset(vblk[:], 0.0).then_inc(consts, 1)
            pool.wait_ge(consts, 2)
            nc.gpsimd.affine_select(out=kmask[:], in_=kmask[:], compare_op=ALU.is_ge, fill=0.0, base=0,
                                    pattern=[[-HD, GH], [0, PRE]], channel_multiplier=1).then_inc(consts, 1)
            pool.wait_ge(consts, 3)
            nc.gpsimd.affine_select(out=kmask[:], in_=kmask[:], compare_op=ALU.is_ge, fill=0.0, base=HD - 1,
                                    pattern=[[HD, GH], [0, PRE]], channel_multiplier=-1).then_inc(consts, 1)
            pool.wait_ge(consts, 4)
            pool.wait_ge(kv_out, G + 2 * B)
            vd = vdup[:].rearrange("p b (g j two c) -> p b g j two c", g=G, j=PG, two=2)
            vb = vblk[:].rearrange("p g (j c) -> p g j c", c=160)
            with pool.Fori(0, B) as b:
                pool.wait_ge(sc_mm, QT * b)
                for g in range(G):
                    k = nc.gpsimd.tensor_tensor(
                        kblk[:, g], kT[:, g, bass.ts(b, PRE)].unsqueeze(1).broadcast_to([P, GH, PRE]), kmask[:],
                        ALU.mult)
                k.then_inc(kblk_ok, 1)
                pool.wait_ge(pj_mm, N_USES * b)
                pool.wait_ge(kblk_ok, b + 1)
                for odd in range(2):
                    if odd:
                        pool.wait_ge(vblk_ok, 2 * b + 1)
                    rows = slice(PRE * odd, PRE * odd + PRE)
                    for g in range(G):
                        v = nc.gpsimd.tensor_copy(vb[rows, g, :, HD * odd:HD * odd + HD],
                                                  vd[rows, b, g, :, odd, :])
                    v.then_inc(vblk_ok, 1)
                pool.wait_ge(vblk_ok, 2 * b + 2)

        @block.tensor
        def _(pe):
            def begin(b, use):
                prev, ago = before(use)
                if not (ago and isinstance(b, int) and b == 0):
                    pe.wait_ge(*taken(b - ago, prev))

            def project(b, use, pairs, cols=S):
                begin(b, use)
                for n, (lhsT, rhs) in enumerate(pairs):
                    mm = nc.tensor.matmul(bank(use)[:, 0:cols], lhsT, rhs, start=n == 0, stop=n == len(pairs) - 1)
                mm.then_inc(pj_mm, 1)

            pe.wait_ge(c_in, 48)
            pe.wait_ge(zeroed, 2)
            for k in range(KC):
                mm = nc.tensor.matmul(pj[0][:, 0:CT], ones_c[:], cT[:, k, :], start=k == 0, stop=k == KC - 1)
            mm.then_inc(c_mm, 1)
            pe.wait_ge(c_act, 1)
            for k in range(KC):
                mm = nc.tensor.matmul(pj[1][:, 0:CT], ones_c[:], cq[:, k, :], start=k == 0, stop=k == KC - 1)
            mm.then_inc(c_mm, 1)
            pe.wait_ge(c_act, 5)
            for g in range(G):
                for k in range(KC):
                    mm = nc.tensor.matmul(pj[g][:, 0:CT], wkv_s[:, k, g * P:g * P + P], cT[:, k, :],
                                          start=k == 0, stop=k == KC - 1)
                mm.then_inc(c_mm, 1)
            for b in range(B):
                for odd in range(2):
                    for k in range(KC):
                        mm = nc.tensor.matmul(sc[b % 2][:].rearrange("p h k -> p (h k)")[
                                                  odd * PRE:odd * PRE + PRE, b // 2 * BANK:b // 2 * BANK + D],
                                              cT[:, k, b * PRE:b * PRE + PRE], wkv_s[:, k, D:2 * D],
                                              start=k == 0, stop=k == KC - 1)
                    mm.then_inc(c_mm, 1)
            pe.wait_ge(kv_out, G + 2 * B)
            pe.wait_ge(w_in, 160)

            def mean_of(t):
                return [(ones[:], t[:, k, :]) for k in range(KD)]

            def scores(b, t):
                if not (isinstance(b, int) and b == 0 and t < 2):
                    pe.wait_ge(shifted, QT * b + t - 1)
                for g in range(G):
                    mm = nc.tensor.matmul(sc[t % 2][:, g * GH:(g + 1) * GH, :].rearrange("p h k -> p (h k)"),
                                          qT[:, g, t * P:t * P + P], kblk[:, g].rearrange("p h k -> p (h k)"),
                                          start=True, stop=True)
                mm.then_inc(sc_mm, 1)

            def turn(b, t):
                pe.wait_ge(att_ok, QT * b + t + 1)
                pe.wait_ge(aT_ok, QT * b + t)
                e = ex[t % 2][:].rearrange("p (j two) k -> p j (two k)", two=2)
                for j in range(PAIRS):
                    mm = nc.tensor.transpose(tp[:, j, :], e[:, j, :], ident[:])
                mm.then_inc(tp_mm, 1)

            def sequence(b):
                pe.wait_ge(sq_ok, 3 * b + 1)
                project(b, "ms", mean_of(sq))
                pe.wait_ge(xh_ok, 3 * b + 1)
                project(b, "mean1", mean_of(x1))
                pe.wait_ge(sq_ok, 3 * b + 2)
                project(b, "var1", mean_of(sq))
                pe.wait_ge(xn_ok, 2 * b + 1)
                for m in range(G):
                    project(b, f"q{m}", [(wq_s[:, k, m * P:m * P + P], xn[:, k, :]) for k in range(KD)])
                pe.wait_ge(*taken(b, f"q{G - 1}"))
                pe.wait_ge(kblk_ok, b + 1)
                scores(b, 0)
                for t in range(QT):
                    if t + 1 < QT:
                        scores(b, t + 1)
                    turn(b, t)
                pe.wait_ge(aT_ok, QT * (b + 1))
                pe.wait_ge(vblk_ok, 2 * (b + 1))
                for g in range(G):
                    project(b, f"o{g}", [(vblk[:, g, P * j:P * j + P], aT[:, g * PG + j, :]) for j in range(PG)])
                pe.wait_ge(*taken(b, f"o{G - 1}"))
                for m in range(KD):
                    project(b, f"p{m}", [(wp_s[:, k, m * P:m * P + P], oT[:, k, :]) for k in range(KD)])
                pe.wait_ge(*taken(b, f"p{KD - 1}"))
                project(b, "mean3", mean_of(x1))
                pe.wait_ge(sq_ok, 3 * b + 3)
                project(b, "var3", mean_of(sq))
                pe.wait_ge(xn_ok, 2 * b + 2)
                for m in range(KH):
                    project(b, f"h{m}", [(w1_s[:, k, m * P:m * P + P], xn[:, k, :]) for k in range(KD)])
                pe.wait_ge(*taken(b, f"h{KH - 1}"))
                for m in range(KD):
                    project(b, f"y{m}", [(w2_s[:, k, m * P:m * P + P], hT[:, k, :]) for k in range(KH)])

            sequence(0)
            with pe.Fori(1, B) as b:
                sequence(b)

        @block.scalar
        def _(act):
            def rstd(b, use, nth):
                act.wait_ge(pj_mm, filled(b, use))
                act.wait_ge(xh_ok, 3 * b + nth)
                nc.scalar.activation(rs[:], bank(use)[:], ACT.Ln, bias=eps[:, 0:1]).then_inc(by_act, 1)
                act.wait_ge(*taken(b, use))
                nc.scalar.activation(rs[:], rs[:], ACT.Exp, scale=-0.5).then_inc(rs_ok, 1)

            def shift(b, nth, ln):
                act.wait_ge(xh_ok, 3 * b + nth)
                for k in range(KD):
                    a = nc.scalar.activation(xn[:, k, :], xm[:, k, :], ACT.Identity,
                                             bias=ln[:, KD + k:KD + k + 1])
                a.then_inc(xn_ok, 1)

            act.wait_ge(c_dve, 1)
            nc.scalar.activation(cq[:], cT[:], ACT.Square).then_inc(c_act, 1)
            act.wait_ge(c_mm, 2)
            nc.scalar.activation(crs[:], pj[1][0:PC, 0:CT], ACT.Ln, bias=eps[0:PC, 0:1]).then_inc(c_act, 1)
            act.wait_ge(c_act, 2)
            nc.scalar.activation(crs[:], crs[:], ACT.Exp, scale=-0.5).then_inc(c_act, 1)
            act.wait_ge(c_dve, 2)
            for k in range(KC):
                nc.scalar.activation(cT[:, k, :], cT[:, k, :], ACT.Identity,
                                     bias=ln2_s[:, KC + k:KC + k + 1]).then_inc(c_act, 1)
            for g in range(G):
                act.wait_ge(c_mm, 3 + g)
                nc.scalar.activation(kT[:, g, :], pj[g][:, 0:CT], ACT.Copy).then_inc(kv_out, 1)
            for b in range(B):
                for odd in range(2):
                    act.wait_ge(c_mm, 2 + G + 2 * b + odd + 1)
                    rows = slice(odd * PRE, odd * PRE + PRE)
                    nc.scalar.activation(vdup[rows, b, :], sc[b % 2][:].rearrange("p h k -> p (h k)")[
                        rows, b // 2 * BANK:b // 2 * BANK + D], ACT.Copy).then_inc(kv_out, 1)
            act.wait_ge(w_in, 160)

            def sequence(b):
                nc.scalar.activation(sq[:], h[:, :, b, PRE:T], ACT.Square).then_inc(sq_ok, 1)
                rstd(b, "ms", 0)
                act.wait_ge(*taken(b, "mean1"))
                nc.scalar.activation(sq[:], xm[:], ACT.Square).then_inc(sq_ok, 1)
                rstd(b, "var1", 1)
                shift(b, 2, ln1_s)
                for m in range(G):
                    act.wait_ge(pj_mm, filled(b, f"q{m}"))
                    nc.scalar.activation(qT[:, m, :], bank(f"q{m}")[:], ACT.Copy).then_inc(by_act, 1)
                for t in range(QT):
                    act.wait_ge(shifted, QT * b + t + 1)
                    nc.scalar.activation(ex[t % 2][:], ex[t % 2][:], ACT.Exp, scale=SCALE).then_inc(ex_ok, 1)
                    if t:
                        unload(b, t - 1)
                unload(b, QT - 1)
                for g in range(G):
                    act.wait_ge(pj_mm, filled(b, f"o{g}"))
                    nc.scalar.activation(oT[:, g, :], bank(f"o{g}")[:], ACT.Copy).then_inc(by_act, 1)
                act.wait_ge(*taken(b, "mean3"))
                nc.scalar.activation(sq[:], xm[:], ACT.Square).then_inc(sq_ok, 1)
                rstd(b, "var3", 2)
                shift(b, 3, ln3_s)
                for m in range(KH):
                    act.wait_ge(pj_mm, filled(b, f"h{m}"))
                    nc.scalar.activation(hT[:, m, :], bank(f"h{m}")[:], ACT.Gelu,
                                         bias=b1_s[:, m:m + 1]).then_inc(by_act, 1)

            def unload(b, t):
                act.wait_ge(tp_mm, QT * b + t + 1)
                nc.scalar.activation(aT[:, :, t * P:t * P + P], tp[:], ACT.Copy).then_inc(aT_ok, 1)

            sequence(0)
            with act.Fori(1, B) as b:
                sequence(b)

        @block.vector
        def _(dve):
            nc.vector.memset(ones_c[:], 1.0 / DC).then_inc(zeroed, 1)
            nc.vector.memset(eps[:], EPS).then_inc(zeroed, 1)
            dve.wait_ge(c_mm, 1)
            nc.vector.tensor_tensor(cT[:], cT[:], pj[0][0:PC, 0:CT].unsqueeze(1).broadcast_to([PC, KC, CT]),
                                    ALU.subtract).then_inc(c_dve, 1)
            dve.wait_ge(c_act, 3)
            dve.wait_ge(c_dve, 1)
            for k in range(KC):
                a = nc.vector.scalar_tensor_tensor(out=cT[:, k, :], in0=cT[:, k, :], scalar=ln2_s[:, k:k + 1],
                                                   in1=crs[:], op0=ALU.mult, op1=ALU.mult)
            a.then_inc(c_dve, 1)
            dve.wait_ge(w_in, 160)

            def scale(b, nth, src, dst, w):
                dve.wait_ge(rs_ok, 3 * b + nth + 1)
                for k in range(KD):
                    a = nc.vector.scalar_tensor_tensor(out=dst(k), in0=src(k), scalar=w[:, k:k + 1], in1=rs[:],
                                                       op0=ALU.mult, op1=ALU.mult)
                return a

            def centre(b, use, nth):
                dve.wait_ge(pj_mm, filled(b, use))
                m = bank(use)[:].unsqueeze(1).broadcast_to([P, KD, S])
                nc.vector.tensor_tensor(xm[:], x1[:], m, ALU.subtract).then_inc(by_dve, 1)

            def sequence(b):
                scale(b, 0, lambda k: h[:, k, b, PRE:T], lambda k: x1[:, k, :], fin_s).then_inc(xh_ok, 1)
                dve.wait_ge(xh_ok, 3 * b + 1)
                centre(b, "mean1", 0)
                dve.wait_ge(*taken(b, "mean1"))
                scale(b, 1, lambda k: xm[:, k, :], lambda k: xm[:, k, :], ln1_s).then_inc(xh_ok, 1)
                for t in range(QT):
                    p = t % 2
                    dve.wait_ge(sc_mm, QT * b + t + 1)
                    nc.vector.tensor_reduce(mx[p][:], sc[p][:], AX_X, ALU.max).then_inc(mx_ok, 1)
                    dve.wait_ge(mx_ok, QT * b + t + 1)
                    if t >= 2:
                        dve.wait_ge(tp_mm, QT * b + t - 1)
                    nc.vector.tensor_tensor(ex[p][:], sc[p][:], mx[p][:].unsqueeze(2).broadcast_to([P, HEADS, PRE]),
                                            ALU.subtract).then_inc(shifted, 1)
                    if t:
                        normalise(b, t - 1)
                normalise(b, QT - 1)
                for m in range(KD):
                    dve.wait_ge(pj_mm, filled(b, f"p{m}"))
                    nc.vector.scalar_tensor_tensor(out=x1[:, m, :], in0=bank(f"p{m}")[:], scalar=bp_s[:, m:m + 1],
                                                   in1=x1[:, m, :], op0=ALU.add, op1=ALU.add).then_inc(by_dve, 1)
                dve.wait_ge(*taken(b, "p1"))
                centre(b, "mean3", 1)
                dve.wait_ge(*taken(b, "mean3"))
                scale(b, 2, lambda k: xm[:, k, :], lambda k: xm[:, k, :], ln3_s).then_inc(xh_ok, 1)
                for m in range(KD):
                    dve.wait_ge(pj_mm, filled(b, f"y{m}"))
                    dve.wait_ge(stored, 16 * (KD * b))
                    nc.vector.scalar_tensor_tensor(out=res[:, m, :], in0=bank(f"y{m}")[:], scalar=b2_s[:, m:m + 1],
                                                   in1=x1[:, m, :], op0=ALU.add, op1=ALU.add).then_inc(by_dve, 1)

            def normalise(b, t):
                p = t % 2
                dve.wait_ge(ex_ok, QT * b + t + 1)
                nc.vector.tensor_reduce(den[p][:], ex[p][:], AX_X, ALU.add).then_inc(den_ok, 1)
                dve.wait_ge(den_ok, QT * b + t + 1)
                nc.vector.reciprocal(den[p][:], den[p][:]).then_inc(rden_ok, 1)
                dve.wait_ge(rden_ok, QT * b + t + 1)
                nc.vector.tensor_tensor(ex[p][:], ex[p][:], den[p][:].unsqueeze(2).broadcast_to([P, HEADS, PRE]),
                                        ALU.mult).then_inc(att_ok, 1)

            sequence(0)
            with dve.Fori(1, B) as b:
                sequence(b)


def kernel(**a):
    import concourse.bacc as bacc
    import numpy as np
    from concourse.bass_utils import run_bass_kernel_spmd

    a = {n: np.asarray(v) for n, v in a.items()}
    m = {n[len("L0_xattn_"):]: v for n, v in a.items() if n.startswith("L0_")}
    t = {n[len("L1_xattn_"):]: v for n, v in a.items() if n.startswith("L1_")}

    def columns(v, p=P):
        return np.moveaxis(v.reshape(*v.shape[:-1], -1, p), -1, 0).reshape(p, -1)

    def per_channel(v):
        return v.reshape(L, ET, P, -1).transpose(2, 0, 1, 3).reshape(P, -1)

    x_w = m["x_proj_w"]
    arrays = {
        "xT": a["x"].transpose(2, 0, 1).reshape(D, B * S),
        "ctxT": a["ctx_768"].transpose(2, 0, 1).reshape(DC, B * PRE),
        "pre_w1": m["pre_w1"], "pre_w2": m["pre_w2"],
        "norm_w": columns(m["norm_w"]),
        "in_w": m["in_proj_w"].transpose(0, 2, 1),
        "conv_w": per_channel(m["conv_w"]), "conv_b": columns(m["conv_b"]),
        "x_w": np.concatenate([x_w[:, R:], x_w[:, :R]], axis=1).transpose(0, 2, 1),
        "dt_w": m["dt_proj_w"].transpose(0, 2, 1), "dt_b": columns(m["dt_proj_b"]),
        "a_log": per_channel(m["A_log"]), "d_skip": columns(m["D_param"]),
        "out_w": m["out_proj_w"].transpose(0, 2, 1),
        "fin_w": columns(m["final_norm_w"]),
        "ln1": columns(np.stack([t["ln1_w"], t["ln1_b"]])),
        "ln2": columns(np.stack([t["ln2_w"], t["ln2_b"]]), PC),
        "ln3": columns(np.stack([t["ln3_w"], t["ln3_b"]])),
        "wq": t["Wq"], "wkv": t["Wkv"], "wproj": t["Wproj"], "bproj": columns(t["bproj"]),
        "w1": t["W1"], "b1": columns(t["b1"]), "w2": t["W2"], "b2": columns(t["b2"]),
    }
    arrays = {n: np.ascontiguousarray(v) for n, v in arrays.items()}
    nc = bacc.Bacc("TRN2", target_bir_lowering=False, num_devices=1)
    args = {n: nc.dram_tensor(n + "_dram", v.shape, mybir.dt.from_np(v.dtype), kind="ExternalInput").ap()
            for n, v in arrays.items()}
    outT = nc.dram_tensor("outT_dram", (KD, B, P, S), F32, kind="ExternalOutput").ap()
    mamba_xattn_kernel(nc, outT=outT, **args)
    r = run_bass_kernel_spmd(nc, [{n + "_dram": v for n, v in arrays.items()}], core_ids=[0])
    got = r.results[0]["outT_dram"]
    return np.ascontiguousarray(got.transpose(1, 3, 0, 2).reshape(B, S, D))
```
